# Optimizing a Trainium2 kernel written in Bass

```python
import numpy as np
import jax
import jax.numpy as jnp

def _softmax(x, axis=-1):
    return jax.nn.softmax(x, axis=axis)

def _gelu(x):
    return jax.nn.gelu(x, approximate=True)

def _silu(x):
    return jax.nn.silu(x)

def _sigmoid(x):
    return jax.nn.sigmoid(x)

def _layernorm(x, axis=-1, eps=1e-05):
    m = jnp.mean(x, axis=axis, keepdims=True)
    v = jnp.var(x, axis=axis, keepdims=True)
    return (x - m) / jnp.sqrt(v + eps)

def _scatter_add(tgt, idx, src, axis=0):
    return tgt.at[idx].add(src)

def _segment_sum(src, seg, n):
    return jax.ops.segment_sum(src, seg, n)
kernel_name = 'mk_dlrm_tower_d1_rec_r8_7f3dee'

def setup_inputs(seed: int=0):
    np.random.seed(seed)
    _w = jnp.asarray

    def _rec_inputs():
        import jax
        import jax.numpy as jnp
        _tk = jax.random.key(seed)
        ids = jnp.stack([jax.random.randint(jax.random.fold_in(_tk, 200 + f), (2048,), 0, v, jnp.int32) for f, v in enumerate([125000, 1000, 12500, 1000, 1000, 1250, 12500, 1250, 12500, 1000, 12500, 1000, 1250, 1250, 12500, 1250, 1250, 1000, 1000, 1250, 1250, 12500, 12500, 1250, 1250, 12500])], axis=1)
        tbl_0 = 0.05 * jax.random.normal(jax.random.fold_in(_tk, 500 + 0), (125000, 128), jnp.float32)
        tbl_1 = 0.05 * jax.random.normal(jax.random.fold_in(_tk, 500 + 1), (1000, 128), jnp.float32)
        tbl_2 = 0.05 * jax.random.normal(jax.random.fold_in(_tk, 500 + 2), (12500, 128), jnp.float32)
        tbl_3 = 0.05 * jax.random.normal(jax.random.fold_in(_tk, 500 + 3), (1000, 128), jnp.float32)
        tbl_4 = 0.05 * jax.random.normal(jax.random.fold_in(_tk, 500 + 4), (1000, 128), jnp.float32)
        tbl_5 = 0.05 * jax.random.normal(jax.random.fold_in(_tk, 500 + 5), (1250, 128), jnp.float32)
        tbl_6 = 0.05 * jax.random.normal(jax.random.fold_in(_tk, 500 + 6), (12500, 128), jnp.float32)
        tbl_7 = 0.05 * jax.random.normal(jax.random.fold_in(_tk, 500 + 7), (1250, 128), jnp.float32)
        tbl_8 = 0.05 * jax.random.normal(jax.random.fold_in(_tk, 500 + 8), (12500, 128), jnp.float32)
        tbl_9 = 0.05 * jax.random.normal(jax.random.fold_in(_tk, 500 + 9), (1000, 128), jnp.float32)
        tbl_10 = 0.05 * jax.random.normal(jax.random.fold_in(_tk, 500 + 10), (12500, 128), jnp.float32)
        tbl_11 = 0.05 * jax.random.normal(jax.random.fold_in(_tk, 500 + 11), (1000, 128), jnp.float32)
        tbl_12 = 0.05 * jax.random.normal(jax.random.fold_in(_tk, 500 + 12), (1250, 128), jnp.float32)
        tbl_13 = 0.05 * jax.random.normal(jax.random.fold_in(_tk, 500 + 13), (1250, 128), jnp.float32)
        tbl_14 = 0.05 * jax.random.normal(jax.random.fold_in(_tk, 500 + 14), (12500, 128), jnp.float32)
        tbl_15 = 0.05 * jax.random.normal(jax.random.fold_in(_tk, 500 + 15), (1250, 128), jnp.float32)
        tbl_16 = 0.05 * jax.random.normal(jax.random.fold_in(_tk, 500 + 16), (1250, 128), jnp.float32)
        tbl_17 = 0.05 * jax.random.normal(jax.random.fold_in(_tk, 500 + 17), (1000, 128), jnp.float32)
        tbl_18 = 0.05 * jax.random.normal(jax.random.fold_in(_tk, 500 + 18), (1000, 128), jnp.float32)
        tbl_19 = 0.05 * jax.random.normal(jax.random.fold_in(_tk, 500 + 19), (1250, 128), jnp.float32)
        tbl_20 = 0.05 * jax.random.normal(jax.random.fold_in(_tk, 500 + 20), (1250, 128), jnp.float32)
        tbl_21 = 0.05 * jax.random.normal(jax.random.fold_in(_tk, 500 + 21), (12500, 128), jnp.float32)
        tbl_22 = 0.05 * jax.random.normal(jax.random.fold_in(_tk, 500 + 22), (12500, 128), jnp.float32)
        tbl_23 = 0.05 * jax.random.normal(jax.random.fold_in(_tk, 500 + 23), (1250, 128), jnp.float32)
        tbl_24 = 0.05 * jax.random.normal(jax.random.fold_in(_tk, 500 + 24), (1250, 128), jnp.float32)
        tbl_25 = 0.05 * jax.random.normal(jax.random.fold_in(_tk, 500 + 25), (12500, 128), jnp.float32)
        _rk = jax.random.fold_in(_tk, 7)
        r_dense_features = -0.000292821 + 1.00034 * jax.random.normal(jax.random.fold_in(_rk, 101), (2048, 128), jnp.float32)
        W_top1 = 0.0405887 * jax.random.normal(jax.random.fold_in(_tk, 801), (607, 512), jnp.float32)
        W_top2 = 0.0441942 * jax.random.normal(jax.random.fold_in(_tk, 802), (512, 256), jnp.float32)
        W_top3 = 0.0625 * jax.random.normal(jax.random.fold_in(_tk, 803), (256, 1), jnp.float32)
        b_top1 = jnp.zeros((512,), jnp.float32)
        b_top2 = jnp.zeros((256,), jnp.float32)
        return (r_dense_features, ids, tbl_0, tbl_1, tbl_2, tbl_3, tbl_4, tbl_5, tbl_6, tbl_7, tbl_8, tbl_9, tbl_10, tbl_11, tbl_12, tbl_13, tbl_14, tbl_15, tbl_16, tbl_17, tbl_18, tbl_19, tbl_20, tbl_21, tbl_22, tbl_23, tbl_24, tbl_25, W_top1, b_top1, W_top2, b_top2, W_top3)
    r_dense_features, ids, tbl_0, tbl_1, tbl_2, tbl_3, tbl_4, tbl_5, tbl_6, tbl_7, tbl_8, tbl_9, tbl_10, tbl_11, tbl_12, tbl_13, tbl_14, tbl_15, tbl_16, tbl_17, tbl_18, tbl_19, tbl_20, tbl_21, tbl_22, tbl_23, tbl_24, tbl_25, W_top1, b_top1, W_top2, b_top2, W_top3 = _rec_inputs()

    def _L0_rec_setup():
        import jax, jax.numpy as jnp
        import numpy as np
        F = 26
        _TRIU_I, _TRIU_J = np.triu_indices(F + 1, k=1)
        key = jax.random.key(seed)
        k1, k2 = jax.random.split(key)
        B, D = (4096, 128)
        dense_features = jax.random.normal(k1, (B, D), dtype=jnp.float32)
        sparse_features = jax.random.normal(k2, (B, F, D), dtype=jnp.float32)
        return {'dense_features': dense_features, 'sparse_features': sparse_features}
    _L0_rec_all = _L0_rec_setup()
    _L0_rec_in = {k: v for k, v in _L0_rec_all.items() if k in ()}
    del _L0_rec_all
    return {'r_dense_features': r_dense_features, 'ids': ids, 'tbl_0': tbl_0, 'tbl_1': tbl_1, 'tbl_2': tbl_2, 'tbl_3': tbl_3, 'tbl_4': tbl_4, 'tbl_5': tbl_5, 'tbl_6': tbl_6, 'tbl_7': tbl_7, 'tbl_8': tbl_8, 'tbl_9': tbl_9, 'tbl_10': tbl_10, 'tbl_11': tbl_11, 'tbl_12': tbl_12, 'tbl_13': tbl_13, 'tbl_14': tbl_14, 'tbl_15': tbl_15, 'tbl_16': tbl_16, 'tbl_17': tbl_17, 'tbl_18': tbl_18, 'tbl_19': tbl_19, 'tbl_20': tbl_20, 'tbl_21': tbl_21, 'tbl_22': tbl_22, 'tbl_23': tbl_23, 'tbl_24': tbl_24, 'tbl_25': tbl_25, 'W_top1': W_top1, 'b_top1': b_top1, 'W_top2': W_top2, 'b_top2': b_top2, 'W_top3': W_top3}

def reference(r_dense_features, ids, tbl_0, tbl_1, tbl_2, tbl_3, tbl_4, tbl_5, tbl_6, tbl_7, tbl_8, tbl_9, tbl_10, tbl_11, tbl_12, tbl_13, tbl_14, tbl_15, tbl_16, tbl_17, tbl_18, tbl_19, tbl_20, tbl_21, tbl_22, tbl_23, tbl_24, tbl_25, W_top1, b_top1, W_top2, b_top2, W_top3):
    import jax
    import jax.numpy as jnp

    def _L0_rec_ref(dense_features, sparse_features):
        import jax, jax.numpy as jnp
        import numpy as np
        F = 26
        _TRIU_I, _TRIU_J = np.triu_indices(F + 1, k=1)
        combined = jnp.concatenate([dense_features[:, None, :], sparse_features], axis=1)
        interactions = jnp.einsum('bfd,bgd->bfg', combined, combined)
        interactions_flat = interactions[:, _TRIU_I, _TRIU_J]
        return jnp.concatenate([dense_features, interactions_flat], axis=1)
    e = jnp.stack([tbl_0[ids[:, 0]], tbl_1[ids[:, 1]], tbl_2[ids[:, 2]], tbl_3[ids[:, 3]], tbl_4[ids[:, 4]], tbl_5[ids[:, 5]], tbl_6[ids[:, 6]], tbl_7[ids[:, 7]], tbl_8[ids[:, 8]], tbl_9[ids[:, 9]], tbl_10[ids[:, 10]], tbl_11[ids[:, 11]], tbl_12[ids[:, 12]], tbl_13[ids[:, 13]], tbl_14[ids[:, 14]], tbl_15[ids[:, 15]], tbl_16[ids[:, 16]], tbl_17[ids[:, 17]], tbl_18[ids[:, 18]], tbl_19[ids[:, 19]], tbl_20[ids[:, 20]], tbl_21[ids[:, 21]], tbl_22[ids[:, 22]], tbl_23[ids[:, 23]], tbl_24[ids[:, 24]], tbl_25[ids[:, 25]]], axis=1)
    z = _L0_rec_ref(r_dense_features, e)
    z = z.reshape(z.shape[0], -1)
    h = jnp.concatenate([z, r_dense_features], axis=1)
    h = jnp.maximum(h @ W_top1 + b_top1, 0.0)
    h = jnp.maximum(h @ W_top2 + b_top2, 0.0)
    y = h @ W_top3
    return y

_drawn_inputs = setup_inputs


def setup_inputs(seed=0):
    import zlib

    import numpy as np

    out = dict(_drawn_inputs(seed))
    spreads = {'b_top1': (0.0, 0.1), 'b_top2': (0.0, 0.1)}
    factors = {}
    for name, (base, spread) in spreads.items():
        noise = np.random.default_rng([zlib.crc32(name.encode()), seed]).standard_normal(out[name].shape)
        drawn = base * np.exp(spread * noise) if base else spread * noise
        out[name] = jnp.asarray(drawn.astype(out[name].dtype))
    for name, factor in factors.items():
        out[name] = (out[name] * factor).astype(out[name].dtype)
    return out
```

```python
import concourse.bass as bass
from concourse import mybir
from contextlib import ExitStack

P = 128
TABLES = 26
F = TABLES + 1
HALF = F // 2
QUAD = 32
FEAT_PITCH = 28
GROUP = 4
GROUPS = -(-F // GROUP)
F_PER_CHUNK = 9
CHUNKS = F // F_PER_CHUNK
CHUNK = F_PER_CHUNK * HALF
G_EXT = F + HALF
BANK = 512


def pair_index(i, j):
    return i * F - i * (i + 1) // 2 + (j - i - 1)


def tower(nc, dense, ids, tables, eye, w1_pairs, w1, b1, w2, b2, w3, out):
    fp32, i32 = mybir.dt.float32, mybir.dt.int32
    ALU = mybir.AluOpType
    ACT = mybir.ActivationFunctionType

    batch, H1, H2 = dense.shape[0], w1.shape[1], w2.shape[1]
    tiles = batch // P
    pairs = tiles // 2
    H1C, H2C = H1 // P, H2 // P
    PAIRS = F * (F - 1) // 2

    dense_v = dense.rearrange("(p t) d -> p t d", t=tiles)
    ids_v = ids.rearrange("(p t) f -> p t f", t=tiles)
    out_v = out.rearrange("(p t) o -> p (t o)", t=tiles)

    ctx = ExitStack()
    with ctx:
        def sb(name, shape, dt=fp32):
            return ctx.enter_context(nc.sbuf_tensor(name, shape, dt))

        def pb(name, shape):
            return ctx.enter_context(nc.psum_tensor(name, shape, fp32))

        def sem(name):
            return ctx.enter_context(nc.semaphore(name))

        idx = sb("idx", [P, 2, TABLES], i32)
        emb = sb("emb", [P, 2, F, P])
        ident = sb("ident", [P, P])
        feats = sb("feats", [P, 2, P, FEAT_PITCH])
        dots = sb("dots", [P, G_EXT * QUAD])
        pair_dots = sb("pair_dots", [P, 2, F, HALF])
        xT = sb("xT", [P, CHUNKS + 1, 2, P])
        w1p_sb = sb("w1p_sb", [CHUNK, CHUNKS, H1])
        w1a_sb = sb("w1a_sb", [P, H1])
        w1b_sb = sb("w1b_sb", [P, H1])
        w1d_sb = sb("w1d_sb", [P, H1])
        w2_sb = sb("w2_sb", [P, H1C, H2])
        w3_sb = sb("w3_sb", [P, H2C])
        b1_sb = sb("b1_sb", [P, H1C])
        b2_sb = sb("b2_sb", [P, H2C])
        h1T = sb("h1T", [P, H1C, 2 * P])
        h2T = sb("h2T", [P, H2C, 2 * P])
        y_sb = sb("y_sb", [P, tiles])

        flip_ps = pb("flip_ps", [P, 2, GROUP, P])
        gram_ps = pb("gram_ps", [P, QUAD, QUAD])
        pairs_ps = pb("pairs_ps", [P, CHUNKS + 1, P])
        mlp_ps = pb("mlp_ps", [P, 2, BANK])

        s_ident = sem("ident_loaded")
        s_weights = sem("weights_loaded")
        s_idx = [sem(f"idx_loaded_{u}") for u in range(2)]
        s_emb = [[sem(f"emb_{u}_{k}") for k in range(GROUPS)] for u in range(2)]
        s_dense = [sem(f"dense_loaded_{u}") for u in range(2)]
        s_free = sem("load_slots_free")
        s_open = sem("gather_slots_open")
        s_zeroed = sem("psum_zeroed")
        s_flip = sem("groups_flipped")
        s_kept = [sem("even_groups_kept"), sem("odd_groups_kept")]
        s_gram = sem("tiles_grammed")
        s_blocks = sem("dots_transposed")
        s_unroll = sem("tiles_unrolled")
        s_pairs = sem("tiles_paired")
        s_xT = sem("tiles_in_xT")
        s_w1d = sem("w1_dense_summed")
        s_mm = sem("mlp_products")
        s_act = sem("mlp_activations")
        s_out = sem("out_stored")

        block = ctx.enter_context(nc.Block())

        def number(i, u, k):
            return 2 * GROUPS * i + GROUPS * u + k

        def kept_before(i, u, k, parity):
            return GROUPS * i + (GROUPS * u + k + 1 - parity) // 2

        def features_in(k):
            return range(GROUP * k, min(GROUP * (k + 1), F))

        def tables_in(k):
            return [f for f in features_in(k) if f]

        STEPS = H1C + H2C + 1

        def once_then_loop(engine, body):
            body(0, True)
            with engine.Fori(1, pairs) as i:
                body(i, False)

        @block.sync
        def _(sp):
            def load_idx(i, u):
                sp.dma_start(idx[:, u:u + 1, :], ids_v[:, bass.ds(2 * i + u, 1), :]).then_inc(s_idx[u], 16)

            def load_dense(i, u):
                sp.dma_start(emb[:, u, 0:1, :], dense_v[:, bass.ds(2 * i + u, 1), :]).then_inc(s_dense[u], 16)

            load_idx(0, 0)
            load_idx(0, 1)
            sp.dma_start(ident[:, :], eye).then_inc(s_ident, 16)
            load_dense(0, 0)
            load_dense(0, 1)
            sp.dma_start(w1p_sb[:, :, :], w1_pairs).then_inc(s_weights, 16)
            sp.dma_start(w1a_sb[:, :], w1[0:P, :]).then_inc(s_weights, 16)
            sp.dma_start(w1b_sb[:, :], w1[P + PAIRS:2 * P + PAIRS, :]).then_inc(s_weights, 16)
            sp.dma_start(w2_sb[:, :, :], w2.rearrange("(c p) n -> p c n", p=P)).then_inc(s_weights, 16)
            sp.dma_start(w3_sb[:, :], w3).then_inc(s_weights, 16)
            sp.dma_start(b1_sb[:, :], b1).then_inc(s_weights, 16)
            sp.dma_start(b2_sb[:, :], b2).then_inc(s_weights, 16)
            with sp.Fori(1, pairs) as i:
                for u in range(2):
                    sp.wait_ge(s_flip, number(i - 1, u, GROUPS))
                    sp.sem_inc(s_free, 1)
                    load_idx(i, u)
                    sp.wait_ge(s_pairs, 2 * i + u - 1)
                    sp.sem_inc(s_free, 1)
                    load_dense(i, u)
            sp.wait_ge(s_act, 1 + STEPS * pairs)
            sp.dma_start(out_v, y_sb[:, :]).then_inc(s_out, 16)
            sp.wait_ge(s_out, 16)

        @block.gpsimd
        def _(pool):
            def body(i, first):
                for u in range(2):
                    pool.wait_ge(s_idx[u], 16 * i + 16)
                    if not first:
                        pool.wait_ge(s_flip, number(i - 1, u, GROUPS))
                    pool.sem_inc(s_open, 1)
                    for k in range(GROUPS):
                        for f in tables_in(k):
                            nc.gpsimd.indirect_dma_start(
                                emb[:, u, f, :], None, tables[f - 1][:, :],
                                bass.IndirectOffsetOnAxis(ap=idx[:, u, f - 1:f], axis=0),
                            ).then_inc(s_emb[u][k], 16)

            once_then_loop(pool, body)

        @block.tensor
        def _(pe):
            def flip(i, u, first):
                for k in range(GROUPS):
                    bank = (GROUPS * u + k) % 2
                    pe.wait_ge(s_emb[u][k], 16 * len(tables_in(k)) * (i + 1))
                    if not first or GROUPS * u + k >= 2:
                        pe.wait_ge(s_kept[bank], kept_before(i, u, k, bank))
                    if k == 0:
                        pe.wait_ge(s_dense[u], 16 * (i + 1))
                    for f in features_in(k):
                        last = nc.tensor.transpose(flip_ps[:, bank, f % GROUP, :], emb[:, u, f, :], ident[:, :])
                    last.then_inc(s_flip, 1)

            def gram(i, u, first):
                for bank in range(2):
                    pe.wait_ge(s_kept[bank], kept_before(i, u, GROUPS, bank))
                if not first or u:
                    pe.wait_ge(s_blocks, 2 * (2 * i + u))
                for n in range(QUAD):
                    for j in range(P // QUAD):
                        row = feats[:, u, QUAD * j + n, 0:F]
                        last = nc.tensor.matmul(gram_ps[QUAD * j:QUAD * j + F, n, 0:F], row, row,
                                                start=True, stop=True)
                last.then_inc(s_gram, 1)

            def pair_rows(i, u, first):
                pe.wait_ge(s_unroll, 2 * i + u + 1)
                if not first:
                    pe.wait_ge(s_xT, 2 * i + u)
                rows = pair_dots[:, u, :, :].rearrange("p f k -> p (f k)")
                for c in range(CHUNKS):
                    nc.tensor.transpose(pairs_ps[0:CHUNK, c, :], rows[:, CHUNK * c:CHUNK * (c + 1)], ident[:, :])
                nc.tensor.transpose(pairs_ps[:, CHUNKS, :], emb[:, u, 0, :], ident[:, :]).then_inc(s_pairs, 1)

            def mlp(i):
                pe.wait_ge(s_xT, 2 * i + 2)
                for q in range(H1C + H2C):
                    bank = mlp_ps[:, q % 2, 0:2 * P]
                    if q != 1:
                        pe.wait_ge(s_act, 1 + STEPS * i + max(q - 1, 0))
                    if q < H1C:
                        for c in range(CHUNKS):
                            nc.tensor.matmul(bank, w1p_sb[:, c, q * P:(q + 1) * P], xT[0:CHUNK, c, :, :],
                                             start=(c == 0), stop=False)
                        last = nc.tensor.matmul(bank, w1d_sb[:, q * P:(q + 1) * P], xT[:, CHUNKS, :, :],
                                                start=False, stop=True)
                    else:
                        if q == H1C:
                            pe.wait_ge(s_act, 1 + STEPS * i + H1C)
                        for c in range(H1C):
                            last = nc.tensor.matmul(bank, w2_sb[:, c, (q - H1C) * P:(q - H1C + 1) * P],
                                                    h1T[:, c, :], start=(c == 0), stop=(c == H1C - 1))
                    last.then_inc(s_mm, 1)
                pe.wait_ge(s_act, 1 + STEPS * i + H1C + H2C)
                for u in range(2):
                    for c in range(H2C):
                        last = nc.tensor.matmul(mlp_ps[:, 0, u:u + 1], h2T[:, c, u * P:(u + 1) * P],
                                                w3_sb[:, c:c + 1], start=(c == 0), stop=(c == H2C - 1))
                last.then_inc(s_mm, 1)

            pe.wait_ge(s_ident, 16)
            pe.wait_ge(s_zeroed, 1)
            flip(0, 0, True)
            gram(0, 0, True)
            flip(0, 1, True)
            pair_rows(0, 0, True)
            gram(0, 1, True)
            pe.wait_ge(s_weights, 16 * 7)
            pe.wait_ge(s_w1d, 1)
            with pe.Fori(1, pairs) as i:
                flip(i, 0, False)
                pair_rows(i - 1, 1, False)
                mlp(i - 1)
                gram(i, 0, False)
                flip(i, 1, False)
                pair_rows(i, 0, False)
                gram(i, 1, False)
            pair_rows(pairs - 1, 1, False)
            mlp(pairs - 1)

        def keep(engine, copy, i, u, bank):
            for k in range(GROUPS):
                if (GROUPS * u + k) % 2 == bank:
                    n = len(features_in(k))
                    engine.wait_ge(s_flip, number(i, u, k) + 1)
                    copy(feats[:, u, :, GROUP * k:GROUP * k + n],
                         flip_ps[:, bank, 0:n, :].rearrange("d f p -> d p f")).then_inc(s_kept[bank], 1)

        @block.vector
        def _(dve):
            def unroll(i, u):
                dve.wait_ge(s_gram, 2 * i + u + 1)
                for g0, n in ((0, F), (F, HALF)):
                    nc.vector.transpose(
                        dots[:, g0 * QUAD:(g0 + n) * QUAD].rearrange("p (g f) -> p g f", f=QUAD),
                        gram_ps[:, :, 0:n].rearrange("p n g -> p g n")).then_inc(s_blocks, 1)
                dve.wait_ge(s_blocks, 2 * (2 * i + u + 1))
                src = bass.AP(tensor=dots, offset=QUAD, ap=[[G_EXT * QUAD, P], [QUAD + 1, F], [QUAD, HALF]])
                nc.vector.tensor_copy(pair_dots[:, u, :, :], src).then_inc(s_unroll, 1)

            def body(i, first):
                for u in range(2):
                    keep(dve, nc.vector.tensor_copy, i, u, 0)
                    unroll(i, u)

            nc.vector.memset(gram_ps[:, :, :], 0.0)
            nc.vector.memset(pairs_ps[:, :, :], 0.0).then_inc(s_zeroed, 1)
            dve.wait_ge(s_weights, 16 * 7)
            nc.vector.tensor_tensor(w1d_sb[:, :], w1a_sb[:, :], w1b_sb[:, :], ALU.add).then_inc(s_w1d, 1)
            once_then_loop(dve, body)

        @block.scalar
        def _(act):
            def keep_pairs(i, u):
                act.wait_ge(s_pairs, 2 * i + u + 1)
                nc.scalar.copy(xT[:, :, u, :], pairs_ps[:, :, :]).then_inc(s_xT, 1)

            def mlp(i):
                for q in range(H1C + H2C):
                    act.wait_ge(s_mm, STEPS * i + q + 1)
                    h, b, c = (h1T, b1_sb, q) if q < H1C else (h2T, b2_sb, q - H1C)
                    nc.scalar.activation(h[:, c, :], mlp_ps[:, q % 2, 0:2 * P], ACT.Relu,
                                         bias=b[:, c:c + 1]).then_inc(s_act, 1)
                act.wait_ge(s_mm, STEPS * (i + 1))
                nc.scalar.copy(y_sb[:, bass.ds(2 * i, 2)], mlp_ps[:, 0, 0:2]).then_inc(s_act, 1)

            act.sem_inc(s_act, 1)
            keep(act, nc.scalar.copy, 0, 0, 1)
            keep(act, nc.scalar.copy, 0, 1, 1)
            keep_pairs(0, 0)
            act.wait_ge(s_weights, 16 * 7)
            with act.Fori(1, pairs) as i:
                keep(act, nc.scalar.copy, i, 0, 1)
                keep_pairs(i - 1, 1)
                mlp(i - 1)
                keep(act, nc.scalar.copy, i, 1, 1)
                keep_pairs(i, 0)
            keep_pairs(pairs - 1, 1)
            mlp(pairs - 1)


def kernel(**inputs):
    import numpy as np
    import concourse.bacc as bacc
    from concourse.bass_utils import run_bass_kernel_spmd

    nc = bacc.Bacc("TRN2", target_bir_lowering=False, num_devices=1)
    arrays = {}

    def dram(name, a):
        a = np.ascontiguousarray(a)
        arrays[name] = a
        return nc.dram_tensor(name, a.shape, mybir.dt.from_np(a.dtype), kind="ExternalInput").ap()

    w1 = np.asarray(inputs["W_top1"])
    order = np.empty((F_PER_CHUNK, HALF, CHUNKS), np.int64)
    for f in range(F):
        for k in range(1, HALF + 1):
            i, j = sorted((f, (f + k) % F))
            order[f % F_PER_CHUNK, k - 1, f // F_PER_CHUNK] = P + pair_index(i, j)
    w1_pairs = w1[order.reshape(CHUNK, CHUNKS)]

    def columns(a):
        return np.asarray(a).reshape(-1, P).T

    dense = dram("dense", inputs["r_dense_features"])
    ids = dram("ids", inputs["ids"])
    tables = [dram(f"tbl_{f}", inputs[f"tbl_{f}"]) for f in range(TABLES)]
    out = nc.dram_tensor("out_y", (dense.shape[0], 1), mybir.dt.float32, kind="ExternalOutput").ap()
    tower(nc, dense, ids, tables, dram("eye", np.eye(P, dtype=np.float32)), dram("w1_pairs", w1_pairs),
          dram("w1", w1), dram("b1", columns(inputs["b_top1"])), dram("w2", inputs["W_top2"]),
          dram("b2", columns(inputs["b_top2"])), dram("w3", columns(inputs["W_top3"])), out)
    r = run_bass_kernel_spmd(nc, [arrays], core_ids=[0])
    return r.results[0]["out_y"]
```

```python
import concourse.bass as bass
from concourse import mybir
from contextlib import ExitStack

P = 128
TABLES = 26
F = TABLES + 1
HALF = F // 2
QUAD = 32
FEAT_PITCH = 28
GROUP = 4
LOOKED_UP = 7
GATHERED = F - LOOKED_UP
GROUPS = -(-GATHERED // GROUP)
LOOK_GROUPS = -(-LOOKED_UP // 2)
MARK_SLOTS = 4
F_PER_CHUNK = 9
CHUNKS = F // F_PER_CHUNK
CHUNK = F_PER_CHUNK * HALF
G_EXT = F + HALF
BANK = 512


def pair_index(i, j):
    return i * F - i * (i + 1) // 2 + (j - i - 1)


def feature_order(table_rows):
    by_size = sorted(range(TABLES), key=lambda t: table_rows[t])
    small = by_size[LOOKED_UP - 1::-1]
    return [t for t in range(TABLES) if t not in small] + small


def row_chunk(rows):
    return max(r for r in range(1, P + 1) if rows % r == 0)


def tower(nc, dense, ids, ids_in_pairs, row_numbers, tables, eye, w1_pairs, w1, b1, w2, b2, w3, out):
    fp32, fp32r, i32 = mybir.dt.float32, mybir.dt.float32r, mybir.dt.int32
    ALU = mybir.AluOpType
    ACT = mybir.ActivationFunctionType

    batch, H1, H2 = dense.shape[0], w1.shape[1], w2.shape[1]
    tiles = batch // P
    pairs = tiles // 2
    H1C, H2C = H1 // P, H2 // P
    PAIRS = F * (F - 1) // 2
    order = feature_order([t.shape[0] for t in tables])
    small = [tables[t] for t in order[GATHERED - 1:]]
    R = [row_chunk(t.shape[0]) for t in small]
    N_CHUNKS = [t.shape[0] // r for t, r in zip(small, R)]
    MAX_CHUNKS = max(N_CHUNKS)

    dense_v = dense.rearrange("(p t) d -> p t d", t=tiles)
    ids_v = ids.rearrange("(p t) f -> p t f", t=tiles)
    out_v = out.rearrange("(p t) o -> p (t o)", t=tiles)

    ctx = ExitStack()
    with ctx:
        def sb(name, shape, dt=fp32):
            return ctx.enter_context(nc.sbuf_tensor(name, shape, dt))

        def pb(name, shape):
            return ctx.enter_context(nc.psum_tensor(name, shape, fp32))

        def sem(name):
            return ctx.enter_context(nc.semaphore(name))

        idx = sb("idx", [P, 2, TABLES], i32)
        emb = sb("emb", [P, 2, GATHERED, P])
        raw = sb("raw", [P, MAX_CHUNKS, P])
        hi = [sb(f"hi_{s}", [P, N_CHUNKS[s], P], fp32r) for s in range(LOOKED_UP)]
        lo = [sb(f"lo_{s}", [P, N_CHUNKS[s], P], fp32r) for s in range(LOOKED_UP)]
        row_no = sb("row_no", [P, LOOKED_UP, MAX_CHUNKS])
        id_cols = sb("id_cols", [P, LOOKED_UP, 2 * P], i32)
        marks = sb("marks", [P, MARK_SLOTS, MAX_CHUNKS, 2 * P], fp32r)
        ident = sb("ident", [P, P])
        feats = sb("feats", [P, 2, P, FEAT_PITCH])
        dots = sb("dots", [P, G_EXT * QUAD])
        pair_dots = sb("pair_dots", [P, 2, F, HALF])
        xT = sb("xT", [P, CHUNKS + 1, 2, P])
        w1p_sb = sb("w1p_sb", [CHUNK, CHUNKS, H1])
        w1a_sb = sb("w1a_sb", [P, H1])
        w1b_sb = sb("w1b_sb", [P, H1])
        w1d_sb = sb("w1d_sb", [P, H1])
        w2_sb = sb("w2_sb", [P, H1C, H2])
        w3_sb = sb("w3_sb", [P, H2C])
        b1_sb = sb("b1_sb", [P, H1C])
        b2_sb = sb("b2_sb", [P, H2C])
        h1T = sb("h1T", [P, H1C, 2 * P])
        h2T = sb("h2T", [P, H2C, 2 * P])
        y_sb = sb("y_sb", [P, tiles])

        places = [raw[:, :, :], dots[:, :].rearrange("p (c d) -> p c d", d=P), h1T[:, :, :].rearrange(
            "p c (u d) -> p (c u) d", d=P), xT[:, :, :, :].rearrange("p c u d -> p (c u) d")]
        PLACES = len(places)

        def waiting(s):
            return places[s % PLACES][0:R[s], 0:N_CHUNKS[s], :]

        flip_ps = pb("flip_ps", [P, 2, GROUP, P])
        gram_ps = pb("gram_ps", [P, QUAD, QUAD])
        pairs_ps = pb("pairs_ps", [P, CHUNKS + 1, P])
        mlp_ps = pb("mlp_ps", [P, 2, BANK])

        s_ident = sem("ident_loaded")
        s_weights = sem("weights_loaded")
        s_raw = [sem(f"raw_table_loaded_{v}") for v in range(4)]
        s_rows = sem("row_numbers_loaded")
        s_cols = sem("id_columns_loaded")
        s_hi = sem("tables_hi")
        s_lo = sem("tables_lo")
        s_marked = sem("tables_marked")
        s_looked = sem("tables_looked_up")
        s_idx = [sem(f"idx_loaded_{u}") for u in range(2)]
        s_emb = [[sem(f"emb_{u}_{k}") for k in range(GROUPS)] for u in range(2)]
        s_dense = [sem(f"dense_loaded_{u}") for u in range(2)]
        s_free = sem("load_slots_free")
        s_open = sem("gather_slots_open")
        s_zeroed = sem("psum_zeroed")
        s_flip = sem("groups_flipped")
        s_kept = [sem("even_groups_kept"), sem("odd_groups_kept")]
        s_gram = sem("tiles_grammed")
        s_blocks = sem("dots_transposed")
        s_unroll = sem("tiles_unrolled")
        s_pairs = sem("tiles_paired")
        s_xT = sem("tiles_in_xT")
        s_w1d = sem("w1_dense_summed")
        s_mm = sem("mlp_products")
        s_act = sem("mlp_activations")
        s_out = sem("out_stored")

        block = ctx.enter_context(nc.Block())

        turns = []
        for k in range(max(GROUPS, LOOK_GROUPS)):
            turns += [("tile0", k)] * (k < GROUPS) + [("look", k)] * (k < LOOK_GROUPS)
        turns += [("tile1", k) for k in range(GROUPS)]
        FLIP = [[turns.index((f"tile{u}", k)) for k in range(GROUPS)] for u in range(2)]
        LOOK = [turns.index(("look", k)) for k in range(LOOK_GROUPS)]
        PER_PAIR = len(turns)
        assert PER_PAIR % 2 == 0

        def kept_before(i, m, bank):
            return PER_PAIR // 2 * i + (m + 1 - bank) // 2

        def features_in(k):
            return range(GROUP * k, min(GROUP * (k + 1), GATHERED))

        def looked_in(k):
            return range(2 * k, min(2 * k + 2, LOOKED_UP))

        def tables_in(k):
            return [f for f in features_in(k) if f]

        STEPS = H1C + H2C + 1

        def once_then_loop(engine, body):
            body(0, True)
            with engine.Fori(1, pairs) as i:
                body(i, False)

        @block.sync
        def _(sp):
            def load_idx(i, u):
                sp.dma_start(idx[:, u:u + 1, :], ids_v[:, bass.ds(2 * i + u, 1), :]).then_inc(s_idx[u], 16)

            def load_dense(i, u):
                sp.dma_start(emb[:, u, 0:1, :], dense_v[:, bass.ds(2 * i + u, 1), :]).then_inc(s_dense[u], 16)

            def load_columns(i):
                sp.dma_start(id_cols[:, :, :], ids_in_pairs[bass.ds(i, 1), :, :].broadcast_to(
                    [P, LOOKED_UP, 2 * P])).then_inc(s_cols, 16)

            load_idx(0, 0)
            load_idx(0, 1)
            load_columns(0)
            sp.dma_start(row_no[:, :, :], row_numbers).then_inc(s_rows, 16)
            sp.dma_start(ident[:, :], eye).then_inc(s_ident, 16)
            load_dense(0, 0)
            load_dense(0, 1)
            for s in range(LOOKED_UP):
                if s >= PLACES:
                    sp.wait_ge(s_lo, s - PLACES + 1)
                sp.dma_start(waiting(s), small[s].rearrange("(p c) d -> p c d", c=N_CHUNKS[s])
                             ).then_inc(s_raw[s % PLACES], 16)
            sp.dma_start(w1p_sb[:, :, :], w1_pairs).then_inc(s_weights, 16)
            sp.dma_start(w1a_sb[:, :], w1[0:P, :]).then_inc(s_weights, 16)
            sp.dma_start(w1b_sb[:, :], w1[P + PAIRS:2 * P + PAIRS, :]).then_inc(s_weights, 16)
            sp.dma_start(w2_sb[:, :, :], w2.rearrange("(c p) n -> p c n", p=P)).then_inc(s_weights, 16)
            sp.dma_start(w3_sb[:, :], w3).then_inc(s_weights, 16)
            sp.dma_start(b1_sb[:, :], b1).then_inc(s_weights, 16)
            sp.dma_start(b2_sb[:, :], b2).then_inc(s_weights, 16)
            with sp.Fori(1, pairs) as i:
                sp.wait_ge(s_marked, LOOKED_UP * i)
                sp.sem_inc(s_free, 1)
                load_columns(i)
                for u in range(2):
                    sp.wait_ge(s_flip, GROUPS * (2 * (i - 1) + u + 1))
                    sp.sem_inc(s_free, 1)
                    load_idx(i, u)
                    sp.wait_ge(s_pairs, 2 * i + u - 1)
                    sp.sem_inc(s_free, 1)
                    load_dense(i, u)
            sp.wait_ge(s_act, 1 + STEPS * pairs)
            sp.dma_start(out_v, y_sb[:, :]).then_inc(s_out, 16)
            sp.wait_ge(s_out, 16)

        @block.gpsimd
        def _(pool):
            def body(i, first):
                for u in range(2):
                    pool.wait_ge(s_idx[u], 16 * i + 16)
                    if not first:
                        pool.wait_ge(s_flip, GROUPS * (2 * (i - 1) + u + 1))
                    pool.sem_inc(s_open, 1)
                    for k in range(GROUPS):
                        for f in tables_in(k):
                            nc.gpsimd.indirect_dma_start(
                                emb[:, u, f, :], None, tables[order[f - 1]][:, :],
                                bass.IndirectOffsetOnAxis(ap=idx[:, u, order[f - 1]:order[f - 1] + 1], axis=0),
                            ).then_inc(s_emb[u][k], 16)

            once_then_loop(pool, body)

        @block.tensor
        def _(pe):
            def flip(i, u, k, first):
                m = FLIP[u][k]
                pe.wait_ge(s_emb[u][k], 16 * len(tables_in(k)) * (i + 1))
                if k == 0:
                    pe.wait_ge(s_dense[u], 16 * (i + 1))
                if not first or m >= 2:
                    pe.wait_ge(s_kept[m % 2], kept_before(i, m, m % 2))
                for f in features_in(k):
                    last = nc.tensor.transpose(flip_ps[:, m % 2, f % GROUP, :], emb[:, u, f, :], ident[:, :])
                last.then_inc(s_flip, 1)

            def look_up(i, k, first):
                m = LOOK[k]
                if not first or m >= 2:
                    pe.wait_ge(s_kept[m % 2], kept_before(i, m, m % 2))
                for s in looked_in(k):
                    if first:
                        pe.wait_ge(s_lo, s + 1)
                    pe.wait_ge(s_marked, LOOKED_UP * i + s + 1)
                    for c in range(N_CHUNKS[s]):
                        for part in (hi, lo):
                            last = nc.tensor.matmul(
                                flip_ps[:, m % 2, 2 * (s % 2):2 * (s % 2) + 2, :], part[s][0:R[s], c, :],
                                marks[0:R[s], s % MARK_SLOTS, c, :], start=(c == 0 and part is hi),
                                stop=(c == N_CHUNKS[s] - 1 and part is lo))
                    last.then_inc(s_looked, 1)

            def gram(i, u, rows, first):
                if rows[0] == 0:
                    for bank in range(2):
                        pe.wait_ge(s_kept[bank], kept_before(i, (FLIP[1][0], PER_PAIR)[u], bank))
                    if not first or u:
                        pe.wait_ge(s_blocks, 2 * (2 * i + u))
                for n in rows:
                    for j in range(P // QUAD):
                        row = feats[:, u, QUAD * j + n, 0:F]
                        last = nc.tensor.matmul(gram_ps[QUAD * j:QUAD * j + F, n, 0:F], row, row,
                                                start=True, stop=True)
                if rows[-1] == QUAD - 1:
                    last.then_inc(s_gram, 1)

            def pair_rows(i, u, first):
                pe.wait_ge(s_unroll, 2 * i + u + 1)
                if not first:
                    pe.wait_ge(s_xT, 2 * i + u)
                rows = pair_dots[:, u, :, :].rearrange("p f k -> p (f k)")
                for c in range(CHUNKS):
                    nc.tensor.transpose(pairs_ps[0:CHUNK, c, :], rows[:, CHUNK * c:CHUNK * (c + 1)], ident[:, :])
                nc.tensor.transpose(pairs_ps[:, CHUNKS, :], emb[:, u, 0, :], ident[:, :]).then_inc(s_pairs, 1)

            def layer(i, q):
                bank = mlp_ps[:, q % 2, 0:2 * P]
                if q != 1:
                    pe.wait_ge(s_act, 1 + STEPS * i + max(q - 1, 0))
                if q < H1C:
                    for c in range(CHUNKS):
                        nc.tensor.matmul(bank, w1p_sb[:, c, q * P:(q + 1) * P], xT[0:CHUNK, c, :, :],
                                         start=(c == 0), stop=False)
                    last = nc.tensor.matmul(bank, w1d_sb[:, q * P:(q + 1) * P], xT[:, CHUNKS, :, :],
                                            start=False, stop=True)
                else:
                    for c in range(H1C):
                        last = nc.tensor.matmul(bank, w2_sb[:, c, (q - H1C) * P:(q - H1C + 1) * P],
                                                h1T[:, c, :], start=(c == 0), stop=(c == H1C - 1))
                last.then_inc(s_mm, 1)

            def first_layer(i):
                pe.wait_ge(s_xT, 2 * i + 2)
                for q in range(H1C):
                    layer(i, q)

            def second_layer(i):
                pe.wait_ge(s_act, 1 + STEPS * i + H1C)
                for q in range(H1C, H1C + H2C):
                    layer(i, q)

            def third_layer(i):
                pe.wait_ge(s_act, 1 + STEPS * i + H1C + H2C)
                for u in range(2):
                    for c in range(H2C):
                        last = nc.tensor.matmul(mlp_ps[:, 0, u:u + 1], h2T[:, c, u * P:(u + 1) * P],
                                                w3_sb[:, c:c + 1], start=(c == 0), stop=(c == H2C - 1))
                last.then_inc(s_mm, 1)

            def body(i, first):
                for k in range(GROUPS):
                    flip(i, 0, k, first)
                    if k < LOOK_GROUPS:
                        look_up(i, k, first)
                    if k == 0 and not first:
                        pair_rows(i - 1, 1, False)
                for k in range(GROUPS):
                    gram(i, 0, range(QUAD * k // GROUPS, QUAD * (k + 1) // GROUPS), first)
                    flip(i, 1, k, first)
                if not first:
                    first_layer(i - 1)
                pair_rows(i, 0, first)
                if not first:
                    second_layer(i - 1)
                gram(i, 1, range(QUAD), first)
                if not first:
                    third_layer(i - 1)

            pe.wait_ge(s_ident, 16)
            pe.wait_ge(s_zeroed, 1)
            body(0, True)
            pe.wait_ge(s_weights, 16 * 7)
            pe.wait_ge(s_w1d, 1)
            with pe.Fori(1, pairs) as i:
                body(i, False)
            pair_rows(pairs - 1, 1, False)
            first_layer(pairs - 1)
            second_layer(pairs - 1)
            third_layer(pairs - 1)

        def keep_flipped(engine, copy, i, u, k):
            m, n = FLIP[u][k], len(features_in(k))
            engine.wait_ge(s_flip, GROUPS * (2 * i + u) + k + 1)
            copy(feats[:, u, :, GROUP * k:GROUP * k + n],
                 flip_ps[:, m % 2, 0:n, :].rearrange("d f p -> d p f")).then_inc(s_kept[m % 2], 1)

        def keep_looked(engine, copy, i, k):
            m, f, n = LOOK[k], GATHERED + 2 * k, len(looked_in(k))
            engine.wait_ge(s_looked, LOOKED_UP * i + 2 * k + n)
            copy(feats[:, :, :, f:f + n].rearrange("d u p f -> d f u p"),
                 flip_ps[:, m % 2, 0:2 * n, :].rearrange("d (f u) p -> d f u p", u=2)).then_inc(s_kept[m % 2], 1)

        @block.vector
        def _(dve):
            def unroll(i, u):
                dve.wait_ge(s_gram, 2 * i + u + 1)
                for g0, n in ((0, F), (F, HALF)):
                    nc.vector.transpose(
                        dots[:, g0 * QUAD:(g0 + n) * QUAD].rearrange("p (g f) -> p g f", f=QUAD),
                        gram_ps[:, :, 0:n].rearrange("p n g -> p g n")).then_inc(s_blocks, 1)
                dve.wait_ge(s_blocks, 2 * (2 * i + u + 1))
                src = bass.AP(tensor=dots, offset=QUAD, ap=[[G_EXT * QUAD, P], [QUAD + 1, F], [QUAD, HALF]])
                nc.vector.tensor_copy(pair_dots[:, u, :, :], src).then_inc(s_unroll, 1)

            def mark(i, s, first):
                if s == 0:
                    dve.wait_ge(s_cols, 16 * i + 16)
                if not (first and s < MARK_SLOTS):
                    dve.wait_ge(s_looked, LOOKED_UP * i + max(s - MARK_SLOTS + 1, 0))
                for c in range(N_CHUNKS[s]):
                    last = nc.vector.tensor_scalar(marks[0:R[s], s % MARK_SLOTS, c, :], id_cols[0:R[s], s, :],
                                                   row_no[0:R[s], s, c:c + 1], None, ALU.is_equal)
                last.then_inc(s_marked, 1)

            def split_lo(s):
                dve.wait_ge(s_hi, s + 1)
                nc.vector.tensor_tensor(lo[s][0:R[s], :, :], waiting(s), hi[s][0:R[s], :, :].bitcast(fp32),
                                        ALU.subtract).then_inc(s_lo, 1)

            def body(i, first, last):
                copy = nc.vector.tensor_copy
                for k in range(GROUPS):
                    keep_flipped(dve, copy, i, 0, k)
                    for s in MARKS_AFTER[k]:
                        if first:
                            split_lo(s)
                        mark(i, s, first)
                for k in range(GROUPS):
                    if FLIP[1][k] % 2 == 0:
                        keep_flipped(dve, copy, i, 1, k)
                unroll(i, 0)
                if not last:
                    for s in range(MARK_SLOTS):
                        mark(i + 1, s, False)
                unroll(i, 1)

            MARKS_AFTER = [[s for s in later if s < LOOKED_UP] for later in ([4], [5, 6], [7], [], [])]

            nc.vector.memset(gram_ps[:, :, :], 0.0)
            nc.vector.memset(pairs_ps[:, :, :], 0.0).then_inc(s_zeroed, 1)
            dve.wait_ge(s_rows, 16)
            for s in range(MARK_SLOTS):
                mark(0, s, True)
                split_lo(s)
            body(0, True, False)
            dve.wait_ge(s_weights, 16 * 7)
            nc.vector.tensor_tensor(w1d_sb[:, :], w1a_sb[:, :], w1b_sb[:, :], ALU.add).then_inc(s_w1d, 1)
            with dve.Fori(1, pairs - 1) as i:
                body(i, False, False)
            body(pairs - 1, False, True)

        @block.scalar
        def _(act):
            def keep_pairs(i, u):
                act.wait_ge(s_pairs, 2 * i + u + 1)
                nc.scalar.copy(xT[:, :, u, :], pairs_ps[:, :, :]).then_inc(s_xT, 1)

            def activate(i, chunks):
                for q in chunks:
                    act.wait_ge(s_mm, STEPS * i + q + 1)
                    h, b, c = (h1T, b1_sb, q) if q < H1C else (h2T, b2_sb, q - H1C)
                    nc.scalar.activation(h[:, c, :], mlp_ps[:, q % 2, 0:2 * P], ACT.Relu,
                                         bias=b[:, c:c + 1]).then_inc(s_act, 1)

            def keep_y(i):
                act.wait_ge(s_mm, STEPS * (i + 1))
                nc.scalar.copy(y_sb[:, bass.ds(2 * i, 2)], mlp_ps[:, 0, 0:2]).then_inc(s_act, 1)

            def body(i, first):
                for k in range(LOOK_GROUPS):
                    keep_looked(act, nc.scalar.copy, i, k)
                    if k == 0 and not first:
                        keep_pairs(i - 1, 1)
                for k in range(GROUPS):
                    if FLIP[1][k] % 2:
                        keep_flipped(act, nc.scalar.copy, i, 1, k)
                if not first:
                    activate(i - 1, range(H1C))
                keep_pairs(i, 0)
                if not first:
                    activate(i - 1, range(H1C, H1C + H2C))
                    keep_y(i - 1)

            act.sem_inc(s_act, 1)
            for s in range(LOOKED_UP):
                act.wait_ge(s_raw[s % PLACES], 16 * (s // PLACES + 1))
                nc.scalar.copy(hi[s][0:R[s], :, :], waiting(s)).then_inc(s_hi, 1)
            body(0, True)
            act.wait_ge(s_weights, 16 * 7)
            with act.Fori(1, pairs) as i:
                body(i, False)
            keep_pairs(pairs - 1, 1)
            activate(pairs - 1, range(H1C + H2C))
            keep_y(pairs - 1)


def kernel(**inputs):
    import numpy as np
    import concourse.bacc as bacc
    from concourse.bass_utils import run_bass_kernel_spmd

    nc = bacc.Bacc("TRN2", target_bir_lowering=False, num_devices=1)
    arrays = {}

    def dram(name, a):
        a = np.ascontiguousarray(a)
        arrays[name] = a
        return nc.dram_tensor(name, a.shape, mybir.dt.from_np(a.dtype), kind="ExternalInput").ap()

    dense = dram("dense", inputs["r_dense_features"])
    ids_a = np.asarray(inputs["ids"])
    ids = dram("ids", ids_a)
    tables = [dram(f"tbl_{f}", inputs[f"tbl_{f}"]) for f in range(TABLES)]
    order = feature_order([t.shape[0] for t in tables])
    small = order[GATHERED - 1:]

    pairs = dense.shape[0] // (2 * P)
    ids_in_pairs = ids_a[:, small].reshape(P, pairs, 2, LOOKED_UP).transpose(1, 3, 2, 0).reshape(
        pairs, LOOKED_UP, 2 * P)
    n_chunks = np.array([tables[t].shape[0] // row_chunk(tables[t].shape[0]) for t in small])
    chunk = np.arange(n_chunks.max())
    row_numbers = (np.arange(P)[:, None, None] * n_chunks[:, None] + chunk).astype(np.float32)

    w1 = np.asarray(inputs["W_top1"])
    place = [0] + [t + 1 for t in order]
    rows = np.empty((F_PER_CHUNK, HALF, CHUNKS), np.int64)
    for f in range(F):
        for k in range(1, HALF + 1):
            i, j = sorted((place[f], place[(f + k) % F]))
            rows[f % F_PER_CHUNK, k - 1, f // F_PER_CHUNK] = P + pair_index(i, j)
    w1_pairs = w1[rows.reshape(CHUNK, CHUNKS)]

    def columns(a):
        return np.asarray(a).reshape(-1, P).T

    out = nc.dram_tensor("out_y", (dense.shape[0], 1), mybir.dt.float32, kind="ExternalOutput").ap()
    tower(nc, dense, ids, dram("ids_in_pairs", ids_in_pairs), dram("row_numbers", row_numbers), tables,
          dram("eye", np.eye(P, dtype=np.float32)), dram("w1_pairs", w1_pairs),
          dram("w1", w1), dram("b1", columns(inputs["b_top1"])), dram("w2", inputs["W_top2"]),
          dram("b2", columns(inputs["b_top2"])), dram("w3", columns(inputs["W_top3"])), out)
    r = run_bass_kernel_spmd(nc, [arrays], core_ids=[0])
    return r.results[0]["out_y"]
```

```python
import concourse.bass as bass
from concourse import mybir
from contextlib import ExitStack

P = 128
TABLES = 26
F = TABLES + 1
HALF = F // 2
QUAD = 32
FEAT_PITCH = 28
GROUP = 4
LOOKED_UP = 7
GATHERED = F - LOOKED_UP
GROUPS = -(-GATHERED // GROUP)
LOOK_GROUPS = -(-LOOKED_UP // 2)
MARK_SLOTS = 4
F_PER_CHUNK = 9
CHUNKS = F // F_PER_CHUNK
CHUNK = F_PER_CHUNK * HALF
G_EXT = F + HALF
BANK = 512


def pair_index(i, j):
    return i * F - i * (i + 1) // 2 + (j - i - 1)


def feature_order(table_rows):
    by_size = sorted(range(TABLES), key=lambda t: table_rows[t])
    small = by_size[LOOKED_UP - 1::-1]
    return [t for t in range(TABLES) if t not in small] + small


def row_chunk(rows):
    return max(r for r in range(1, P + 1) if rows % r == 0)


def tower(nc, dense, ids, ids_in_pairs, row_numbers, tables, eye, w1_pairs, w1, b1, w2, b2, w3, out):
    fp32, fp32r, i32 = mybir.dt.float32, mybir.dt.float32r, mybir.dt.int32
    ALU = mybir.AluOpType
    ACT = mybir.ActivationFunctionType

    batch, H1, H2 = dense.shape[0], w1.shape[1], w2.shape[1]
    tiles = batch // P
    pairs = tiles // 2
    H1C, H2C = H1 // P, H2 // P
    PAIRS = F * (F - 1) // 2
    order = feature_order([t.shape[0] for t in tables])
    small = [tables[t] for t in order[GATHERED - 1:]]
    R = [row_chunk(t.shape[0]) for t in small]
    N_CHUNKS = [t.shape[0] // r for t, r in zip(small, R)]
    MAX_CHUNKS = max(N_CHUNKS)

    dense_v = dense.rearrange("(p t) d -> p t d", t=tiles)
    ids_v = ids.rearrange("(p t) f -> p t f", t=tiles)
    out_v = out.rearrange("(p t) o -> o p t", t=tiles)

    ctx = ExitStack()
    with ctx:
        def sb(name, shape, dt=fp32):
            return ctx.enter_context(nc.sbuf_tensor(name, shape, dt))

        def pb(name, shape):
            return ctx.enter_context(nc.psum_tensor(name, shape, fp32))

        def sem(name):
            return ctx.enter_context(nc.semaphore(name))

        idx = sb("idx", [P, 2, TABLES], i32)
        emb = sb("emb", [P, 2, GATHERED, P])
        raw_then_y = sb("raw_then_y", [P, max(MAX_CHUNKS, tiles) * P])
        hi = [sb(f"hi_{s}", [P, N_CHUNKS[s], P], fp32r) for s in range(LOOKED_UP)]
        lo = [sb(f"lo_{s}", [P, N_CHUNKS[s], P], fp32r) for s in range(LOOKED_UP)]
        row_no = sb("row_no", [P, LOOKED_UP, MAX_CHUNKS])
        id_cols = sb("id_cols", [P, LOOKED_UP, 2 * P], i32)
        marks = sb("marks", [P, MARK_SLOTS, MAX_CHUNKS, 2 * P], fp32r)
        ident = sb("ident", [P, P])
        feats = sb("feats", [P, 2, P, FEAT_PITCH])
        dots = sb("dots", [P, G_EXT * QUAD])
        pair_dots = sb("pair_dots", [P, 2, F, HALF])
        xT = sb("xT", [P, CHUNKS + 1, 2, P])
        w1p_sb = sb("w1p_sb", [CHUNK, CHUNKS, H1])
        w1a_sb = sb("w1a_sb", [P, H1])
        w1b_sb = sb("w1b_sb", [P, H1])
        w1d_sb = sb("w1d_sb", [P, H1])
        w2_sb = sb("w2_sb", [P, H1C, H2])
        w3_sb = sb("w3_sb", [P, H2C])
        b1_sb = sb("b1_sb", [P, H1C])
        b2_sb = sb("b2_sb", [P, H2C])
        h1T = sb("h1T", [P, H1C, 2 * P])
        h2T = sb("h2T", [P, H2C, 2 * P])

        places = [raw_then_y[:, 0:MAX_CHUNKS * P].rearrange("p (c d) -> p c d", d=P),
                  dots[:, :].rearrange("p (c d) -> p c d", d=P),
                  h1T[:, :, :].rearrange("p c (u d) -> p (c u) d", d=P),
                  xT[:, :, :, :].rearrange("p c u d -> p (c u) d")]
        PLACES = len(places)
        y_sb = raw_then_y[0:1, 0:P * tiles].rearrange("o (p t) -> o p t", t=tiles)

        def waiting(s):
            return places[s % PLACES][0:R[s], 0:N_CHUNKS[s], :]

        flip_ps = pb("flip_ps", [P, 2, GROUP, P])
        gram_ps = pb("gram_ps", [P, QUAD, QUAD])
        pairs_ps = pb("pairs_ps", [P, CHUNKS, P])
        mlp_ps = pb("mlp_ps", [P, 2, BANK])

        s_ident = sem("ident_loaded")
        s_weights = sem("weights_loaded")
        s_raw = [sem(f"raw_table_loaded_{v}") for v in range(4)]
        s_rows = sem("row_numbers_loaded")
        s_cols = sem("id_columns_loaded")
        s_hi = sem("tables_hi")
        s_lo = sem("tables_lo")
        s_marked = sem("tables_marked")
        s_looked = sem("tables_looked_up")
        s_idx = [sem(f"idx_loaded_{u}") for u in range(2)]
        s_emb = [[sem(f"emb_{u}_{k}") for k in range(GROUPS)] for u in range(2)]
        s_dense = [sem(f"dense_loaded_{u}") for u in range(2)]
        s_free = sem("load_slots_free")
        s_open = sem("gather_slots_open")
        s_zeroed = sem("psum_zeroed")
        s_flip = sem("groups_flipped")
        s_kept = [sem("even_groups_kept"), sem("odd_groups_kept")]
        s_gram = sem("tiles_grammed")
        s_blocks = sem("dots_transposed")
        s_unroll = sem("tiles_unrolled")
        s_pairs = sem("tiles_paired")
        s_xT = sem("tiles_in_xT")
        s_w1d = sem("w1_dense_summed")
        s_mm = sem("mlp_products")
        s_act = sem("mlp_activations")
        s_out = sem("out_stored")

        block = ctx.enter_context(nc.Block())

        turns = []
        for k in range(max(GROUPS, LOOK_GROUPS)):
            turns += [("tile0", k)] * (k < GROUPS) + [("look", k)] * (k < LOOK_GROUPS)
        turns += [("tile1", k) for k in range(GROUPS)]
        FLIP = [[turns.index((f"tile{u}", k)) for k in range(GROUPS)] for u in range(2)]
        LOOK = [turns.index(("look", k)) for k in range(LOOK_GROUPS)]
        PER_PAIR = len(turns)
        assert PER_PAIR % 2 == 0

        def kept_before(i, m, bank):
            return PER_PAIR // 2 * i + (m + 1 - bank) // 2

        def features_in(k):
            return range(GROUP * k, min(GROUP * (k + 1), GATHERED))

        def looked_in(k):
            return range(2 * k, min(2 * k + 2, LOOKED_UP))

        def tables_in(k):
            return [f for f in features_in(k) if f]

        FIRST_BEFORE_LOOK = [[], [], [0], [1]]
        FIRST_LATER = [2, 3]
        assert GROUPS == 5 and LOOK_GROUPS == 4 and H1C == 4

        STEPS = H1C + H2C + 1
        BOTH = range(2)
        LAST = [(pairs - 1 + u, range(u, u + 1)) for u in range(2)]

        def cols(us):
            return slice(us[0] * P, (us[-1] + 1) * P)

        @block.sync
        def _(sp):
            def load_idx(i, u):
                sp.dma_start(idx[:, u:u + 1, :], ids_v[:, bass.ds(2 * i + u, 1), :]).then_inc(s_idx[u], 16)

            def load_dense(i, u):
                sp.dma_start(emb[:, u, 0:1, :], dense_v[:, bass.ds(2 * i + u, 1), :]).then_inc(s_dense[u], 16)

            def load_columns(i):
                sp.dma_start(id_cols[:, :, :], ids_in_pairs[bass.ds(i, 1), :, :].broadcast_to(
                    [P, LOOKED_UP, 2 * P])).then_inc(s_cols, 16)

            load_idx(0, 0)
            load_idx(0, 1)
            load_columns(0)
            sp.dma_start(row_no[:, :, :], row_numbers).then_inc(s_rows, 16)
            sp.dma_start(ident[:, :], eye).then_inc(s_ident, 16)
            load_dense(0, 0)
            load_dense(0, 1)
            for s in range(LOOKED_UP):
                if s >= PLACES:
                    sp.wait_ge(s_lo, s - PLACES + 1)
                sp.dma_start(waiting(s), small[s].rearrange("(p c) d -> p c d", c=N_CHUNKS[s])
                             ).then_inc(s_raw[s % PLACES], 16)
            sp.dma_start(w1p_sb[:, :, :], w1_pairs).then_inc(s_weights, 16)
            sp.dma_start(w1a_sb[:, :], w1[0:P, :]).then_inc(s_weights, 16)
            sp.dma_start(w1b_sb[:, :], w1[P + PAIRS:2 * P + PAIRS, :]).then_inc(s_weights, 16)
            sp.dma_start(w2_sb[:, :, :], w2.rearrange("(c p) n -> p c n", p=P)).then_inc(s_weights, 16)
            sp.dma_start(w3_sb[:, :], w3).then_inc(s_weights, 16)
            sp.dma_start(b1_sb[:, :], b1).then_inc(s_weights, 16)
            sp.dma_start(b2_sb[:, :], b2).then_inc(s_weights, 16)
            with sp.Fori(1, pairs) as i:
                sp.wait_ge(s_marked, LOOKED_UP * i)
                sp.sem_inc(s_free, 1)
                load_columns(i)
                for u in range(2):
                    sp.wait_ge(s_flip, GROUPS * (2 * (i - 1) + u + 1))
                    sp.sem_inc(s_free, 1)
                    load_idx(i, u)
                    load_dense(i, u)
            sp.wait_ge(s_act, 1 + STEPS * (pairs + 1))
            sp.dma_start(out_v, y_sb[:, :, :]).then_inc(s_out, 16)
            sp.wait_ge(s_out, 16)

        @block.gpsimd
        def _(pool):
            def body(i, first):
                for u in range(2):
                    pool.wait_ge(s_idx[u], 16 * i + 16)
                    if not first:
                        pool.wait_ge(s_flip, GROUPS * (2 * (i - 1) + u + 1))
                    pool.sem_inc(s_open, 1)
                    for k in range(GROUPS):
                        for f in tables_in(k):
                            nc.gpsimd.indirect_dma_start(
                                emb[:, u, f, :], None, tables[order[f - 1]][:, :],
                                bass.IndirectOffsetOnAxis(ap=idx[:, u, order[f - 1]:order[f - 1] + 1], axis=0),
                            ).then_inc(s_emb[u][k], 16)

            body(0, True)
            with pool.Fori(1, pairs) as i:
                body(i, False)

        @block.tensor
        def _(pe):
            def flip(i, u, k, first):
                m = FLIP[u][k]
                pe.wait_ge(s_emb[u][k], 16 * len(tables_in(k)) * (i + 1))
                if k == 0:
                    pe.wait_ge(s_dense[u], 16 * (i + 1))
                if not first or m >= 2:
                    pe.wait_ge(s_kept[m % 2], kept_before(i, m, m % 2))
                for f in features_in(k):
                    last = nc.tensor.transpose(flip_ps[:, m % 2, f % GROUP, :], emb[:, u, f, :], ident[:, :])
                last.then_inc(s_flip, 1)

            def look_up(i, k, first):
                m = LOOK[k]
                if not first or m >= 2:
                    pe.wait_ge(s_kept[m % 2], kept_before(i, m, m % 2))
                for s in looked_in(k):
                    if first:
                        pe.wait_ge(s_lo, s + 1)
                    pe.wait_ge(s_marked, LOOKED_UP * i + s + 1)
                    for c in range(N_CHUNKS[s]):
                        for part in (hi, lo):
                            last = nc.tensor.matmul(
                                flip_ps[:, m % 2, 2 * (s % 2):2 * (s % 2) + 2, :], part[s][0:R[s], c, :],
                                marks[0:R[s], s % MARK_SLOTS, c, :], start=(c == 0 and part is hi),
                                stop=(c == N_CHUNKS[s] - 1 and part is lo))
                    last.then_inc(s_looked, 1)

            def gram(i, u, rows, first):
                if rows[0] == 0:
                    for bank in range(2):
                        pe.wait_ge(s_kept[bank], kept_before(i, (FLIP[1][0], PER_PAIR)[u], bank))
                    if not first or u:
                        pe.wait_ge(s_blocks, 2 * (2 * i + u))
                for n in rows:
                    for j in range(P // QUAD):
                        row = feats[:, u, QUAD * j + n, 0:F]
                        last = nc.tensor.matmul(gram_ps[QUAD * j:QUAD * j + F, n, 0:F], row, row,
                                                start=True, stop=True)
                if rows[-1] == QUAD - 1:
                    last.then_inc(s_gram, 1)

            def pair_rows(i, u, first):
                pe.wait_ge(s_unroll, 2 * i + u + 1)
                if not first:
                    pe.wait_ge(s_xT, 2 * (2 * i + u))
                rows = pair_dots[:, u, :, :].rearrange("p f k -> p (f k)")
                for c in range(CHUNKS):
                    last = nc.tensor.transpose(pairs_ps[0:CHUNK, c, :], rows[:, CHUNK * c:CHUNK * (c + 1)],
                                               ident[:, :])
                last.then_inc(s_pairs, 1)

            def layer(i, us, q):
                bank = mlp_ps[:, q % 2, 0:len(us) * P]
                if q != 1:
                    pe.wait_ge(s_act, 1 + STEPS * i + max(q - 1, 0))
                if q < H1C:
                    for c in range(CHUNKS):
                        nc.tensor.matmul(bank, w1p_sb[:, c, q * P:(q + 1) * P],
                                         xT[0:CHUNK, c, us[0]:us[-1] + 1, :], start=(c == 0), stop=False)
                    last = nc.tensor.matmul(bank, w1d_sb[:, q * P:(q + 1) * P],
                                            xT[:, CHUNKS, us[0]:us[-1] + 1, :], start=False, stop=True)
                else:
                    for c in range(H1C):
                        if q == H1C:
                            pe.wait_ge(s_act, 1 + STEPS * i + c + 1)
                        last = nc.tensor.matmul(bank, w2_sb[:, c, (q - H1C) * P:(q - H1C + 1) * P],
                                                h1T[:, c, cols(us)], start=(c == 0), stop=(c == H1C - 1))
                last.then_inc(s_mm, 1)

            def first_layer(i, us, tiles_before, chunks=range(H1C)):
                for q in chunks:
                    if q == 0:
                        pe.wait_ge(s_xT, 2 * (tiles_before + len(us)))
                    layer(i, us, q)

            def second_layer(i, us):
                for q in range(H1C, H1C + H2C):
                    layer(i, us, q)

            def third_layer(i, us):
                for c in range(H2C):
                    pe.wait_ge(s_act, 1 + STEPS * i + H1C + c + 1)
                    last = nc.tensor.matmul(mlp_ps[0:1, 0, 0:len(us) * P], w3_sb[:, c:c + 1], h2T[:, c, cols(us)],
                                            start=(c == 0), stop=(c == H2C - 1))
                last.then_inc(s_mm, 1)

            def tile0_and_look_up(i, first):
                for k in range(GROUPS):
                    if k == GROUPS - 1 and not first:
                        first_layer(i - 1, BOTH, 2 * (i - 1), FIRST_LATER[0:1])
                    flip(i, 0, k, first)
                    if not first:
                        first_layer(i - 1, BOTH, 2 * (i - 1),
                                    FIRST_BEFORE_LOOK[k] if k < GROUPS - 1 else FIRST_LATER[1:])
                    if k < LOOK_GROUPS:
                        look_up(i, k, first)
                    if k == 0 and not first:
                        pair_rows(i - 1, 1, False)

            def gram0_and_flips(i, groups, first):
                for k in range(groups):
                    gram(i, 0, range(QUAD * k // groups, QUAD * (k + 1) // groups), first)
                    flip(i, 1, k, first)

            def body(i, first):
                tile0_and_look_up(i, first)
                gram0_and_flips(i, GROUPS - 1, first)
                if first:
                    flip(i, 1, GROUPS - 1, True)
                    gram(i, 1, range(QUAD), True)
                    pair_rows(i, 0, True)
                else:
                    second_layer(i - 1, BOTH)
                    pair_rows(i, 0, False)
                    flip(i, 1, GROUPS - 1, False)
                    third_layer(i - 1, BOTH)
                    gram(i, 1, range(QUAD), False)

            def last_pair(i):
                tile0_and_look_up(i, False)
                gram0_and_flips(i, GROUPS - 2, False)
                second_layer(i - 1, BOTH)
                pair_rows(i, 0, False)
                third_layer(i - 1, BOTH)
                flip(i, 1, GROUPS - 2, False)
                first_layer(*LAST[0], 2 * i, range(H1C // 2))
                flip(i, 1, GROUPS - 1, False)
                first_layer(*LAST[0], 2 * i, range(H1C // 2, H1C))
                gram(i, 1, range(QUAD), False)
                second_layer(*LAST[0])
                third_layer(*LAST[0])
                pair_rows(i, 1, False)
                first_layer(*LAST[1], 2 * i + 1)
                second_layer(*LAST[1])
                third_layer(*LAST[1])

            pe.wait_ge(s_ident, 16)
            pe.wait_ge(s_zeroed, 1)
            body(0, True)
            pe.wait_ge(s_weights, 16 * 7)
            pe.wait_ge(s_w1d, 1)
            with pe.Fori(1, pairs - 1) as i:
                body(i, False)
            last_pair(pairs - 1)

        def keep_flipped(engine, copy, i, u, k):
            m, n = FLIP[u][k], len(features_in(k))
            engine.wait_ge(s_flip, GROUPS * (2 * i + u) + k + 1)
            copy(feats[:, u, :, GROUP * k:GROUP * k + n],
                 flip_ps[:, m % 2, 0:n, :].rearrange("d f p -> d p f")).then_inc(s_kept[m % 2], 1)

        def keep_looked(engine, copy, i, k):
            m, f, n = LOOK[k], GATHERED + 2 * k, len(looked_in(k))
            engine.wait_ge(s_looked, LOOKED_UP * i + 2 * k + n)
            copy(feats[:, :, :, f:f + n].rearrange("d u p f -> d f u p"),
                 flip_ps[:, m % 2, 0:2 * n, :].rearrange("d (f u) p -> d f u p", u=2)).then_inc(s_kept[m % 2], 1)

        @block.vector
        def _(dve):
            def unroll(i, u, first=False):
                dve.wait_ge(s_gram, 2 * i + u + 1)
                if not first or u:
                    dve.wait_ge(s_unroll, 2 * i + u)
                for g0, n in ((0, F), (F, HALF)):
                    nc.vector.transpose(
                        dots[:, g0 * QUAD:(g0 + n) * QUAD].rearrange("p (g f) -> p g f", f=QUAD),
                        gram_ps[:, :, 0:n].rearrange("p n g -> p g n")).then_inc(s_blocks, 1)
                dve.wait_ge(s_blocks, 2 * (2 * i + u + 1))
                src = bass.AP(tensor=dots, offset=QUAD, ap=[[G_EXT * QUAD, P], [QUAD + 1, F], [QUAD, HALF]])
                nc.vector.tensor_copy(pair_dots[:, u, :, :], src).then_inc(s_unroll, 1)

            def mark(i, s, first):
                if s == 0:
                    dve.wait_ge(s_cols, 16 * i + 16)
                if not (first and s < MARK_SLOTS):
                    dve.wait_ge(s_looked, LOOKED_UP * i + max(s - MARK_SLOTS + 1, 0))
                for c in range(N_CHUNKS[s]):
                    last = nc.vector.tensor_scalar(marks[0:R[s], s % MARK_SLOTS, c, :], id_cols[0:R[s], s, :],
                                                   row_no[0:R[s], s, c:c + 1], None, ALU.is_equal)
                last.then_inc(s_marked, 1)

            def split_lo(s):
                dve.wait_ge(s_hi, s + 1)
                nc.vector.tensor_tensor(lo[s][0:R[s], :, :], waiting(s), hi[s][0:R[s], :, :].bitcast(fp32),
                                        ALU.subtract).then_inc(s_lo, 1)

            def keep_even(i, groups):
                for k in groups:
                    if FLIP[1][k] % 2 == 0:
                        keep_flipped(dve, nc.vector.tensor_copy, i, 1, k)

            def body(i, first, last):
                if not first:
                    dve.wait_ge(s_xT, 2 * (2 * i - 1))
                for k in range(GROUPS):
                    keep_flipped(dve, nc.vector.tensor_copy, i, 0, k)
                    for s in MARKS_AFTER[k]:
                        if first:
                            split_lo(s)
                        mark(i, s, first)
                keep_even(i, range(GROUPS - 2))
                if last:
                    unroll(i, 0)
                keep_even(i, range(GROUPS - 2, GROUPS))
                if not last:
                    unroll(i, 0, first)
                if first:
                    dve.wait_ge(s_weights, 16 * 7)
                    nc.vector.tensor_tensor(w1d_sb[:, :], w1a_sb[:, :], w1b_sb[:, :], ALU.add).then_inc(s_w1d, 1)
                if not last:
                    for s in range(MARK_SLOTS):
                        mark(i + 1, s, False)
                unroll(i, 1)

            MARKS_AFTER = [[s for s in later if s < LOOKED_UP] for later in ([4], [5, 6], [7], [], [])]

            nc.vector.memset(gram_ps[:, :, :], 0.0).then_inc(s_zeroed, 1)
            dve.wait_ge(s_rows, 16)
            for s in range(MARK_SLOTS):
                mark(0, s, True)
                split_lo(s)
            body(0, True, False)
            with dve.Fori(1, pairs - 1) as i:
                body(i, False, False)
            body(pairs - 1, False, True)

        @block.scalar
        def _(act):
            def keep_pairs(i, u):
                act.wait_ge(s_gram, 2 * i + u + 1)
                nc.scalar.copy(xT[:, CHUNKS, u, :], feats[:, u, :, 0]).then_inc(s_xT, 1)
                act.wait_ge(s_pairs, 2 * i + u + 1)
                nc.scalar.copy(xT[0:CHUNK, 0:CHUNKS, u, :], pairs_ps[0:CHUNK, :, :]).then_inc(s_xT, 1)

            def activate(i, us, chunks):
                for q in chunks:
                    act.wait_ge(s_mm, STEPS * i + q + 1)
                    h, b, c = (h1T, b1_sb, q) if q < H1C else (h2T, b2_sb, q - H1C)
                    nc.scalar.activation(h[:, c, cols(us)], mlp_ps[:, q % 2, 0:len(us) * P], ACT.Relu,
                                         bias=b[:, c:c + 1]).then_inc(s_act, 1)

            def keep_y(i, us, tiles_before):
                act.wait_ge(s_mm, STEPS * (i + 1))
                nc.scalar.copy(y_sb[:, :, bass.ds(tiles_before, len(us))].rearrange("o p u -> o u p"),
                               mlp_ps[0:1, 0, 0:len(us) * P].rearrange("o (u p) -> o u p", u=len(us))
                               ).then_inc(s_act, 1)

            FIRST_LAYER, SECOND_LAYER = range(H1C), range(H1C, H1C + H2C)

            def keep_odd(i, groups):
                for k in groups:
                    if FLIP[1][k] % 2:
                        keep_flipped(act, nc.scalar.copy, i, 1, k)

            def look_up_and_first_layer(i, first):
                for k in range(LOOK_GROUPS):
                    if not first:
                        activate(i - 1, BOTH, FIRST_BEFORE_LOOK[k])
                    keep_looked(act, nc.scalar.copy, i, k)
                    if k == 0 and not first:
                        keep_pairs(i - 1, 1)
                if not first:
                    activate(i - 1, BOTH, FIRST_LATER)

            def body(i, first):
                look_up_and_first_layer(i, first)
                keep_odd(i, range(GROUPS - 1))
                if first:
                    keep_odd(i, range(GROUPS - 1, GROUPS))
                    keep_pairs(i, 0)
                else:
                    activate(i - 1, BOTH, SECOND_LAYER)
                    keep_pairs(i, 0)
                    keep_odd(i, range(GROUPS - 1, GROUPS))
                    keep_y(i - 1, BOTH, 2 * (i - 1))

            def last_pair(i):
                look_up_and_first_layer(i, False)
                keep_odd(i, range(GROUPS - 2))
                activate(i - 1, BOTH, SECOND_LAYER)
                keep_pairs(i, 0)
                keep_y(i - 1, BOTH, 2 * (i - 1))
                keep_odd(i, range(GROUPS - 2, GROUPS - 1))
                activate(*LAST[0], FIRST_LAYER[:H1C // 2])
                keep_odd(i, range(GROUPS - 1, GROUPS))
                activate(*LAST[0], FIRST_LAYER[H1C // 2:])
                activate(*LAST[0], SECOND_LAYER)
                keep_y(*LAST[0], 2 * i)
                keep_pairs(i, 1)
                activate(*LAST[1], FIRST_LAYER)
                activate(*LAST[1], SECOND_LAYER)
                keep_y(*LAST[1], 2 * i + 1)

            act.sem_inc(s_act, 1)
            for s in range(LOOKED_UP):
                act.wait_ge(s_raw[s % PLACES], 16 * (s // PLACES + 1))
                nc.scalar.copy(hi[s][0:R[s], :, :], waiting(s)).then_inc(s_hi, 1)
            body(0, True)
            act.wait_ge(s_weights, 16 * 7)
            with act.Fori(1, pairs - 1) as i:
                body(i, False)
            last_pair(pairs - 1)


def kernel(**inputs):
    import numpy as np
    import concourse.bacc as bacc
    from concourse.bass_utils import run_bass_kernel_spmd

    nc = bacc.Bacc("TRN2", target_bir_lowering=False, num_devices=1)
    arrays = {}

    def dram(name, a):
        a = np.ascontiguousarray(a)
        arrays[name] = a
        return nc.dram_tensor(name, a.shape, mybir.dt.from_np(a.dtype), kind="ExternalInput").ap()

    dense = dram("dense", inputs["r_dense_features"])
    ids_a = np.asarray(inputs["ids"])
    ids = dram("ids", ids_a)
    tables = [dram(f"tbl_{f}", inputs[f"tbl_{f}"]) for f in range(TABLES)]
    order = feature_order([t.shape[0] for t in tables])
    small = order[GATHERED - 1:]

    pairs = dense.shape[0] // (2 * P)
    ids_in_pairs = ids_a[:, small].reshape(P, pairs, 2, LOOKED_UP).transpose(1, 3, 2, 0).reshape(
        pairs, LOOKED_UP, 2 * P)
    n_chunks = np.array([tables[t].shape[0] // row_chunk(tables[t].shape[0]) for t in small])
    chunk = np.arange(n_chunks.max())
    row_numbers = (np.arange(P)[:, None, None] * n_chunks[:, None] + chunk).astype(np.float32)

    w1 = np.asarray(inputs["W_top1"])
    place = [0] + [t + 1 for t in order]
    rows = np.empty((F_PER_CHUNK, HALF, CHUNKS), np.int64)
    for f in range(F):
        for k in range(1, HALF + 1):
            i, j = sorted((place[f], place[(f + k) % F]))
            rows[f % F_PER_CHUNK, k - 1, f // F_PER_CHUNK] = P + pair_index(i, j)
    w1_pairs = w1[rows.reshape(CHUNK, CHUNKS)]

    def columns(a):
        return np.asarray(a).reshape(-1, P).T

    out = nc.dram_tensor("out_y", (dense.shape[0], 1), mybir.dt.float32, kind="ExternalOutput").ap()
    tower(nc, dense, ids, dram("ids_in_pairs", ids_in_pairs), dram("row_numbers", row_numbers), tables,
          dram("eye", np.eye(P, dtype=np.float32)), dram("w1_pairs", w1_pairs),
          dram("w1", w1), dram("b1", columns(inputs["b_top1"])), dram("w2", inputs["W_top2"]),
          dram("b2", columns(inputs["b_top2"])), dram("w3", columns(inputs["W_top3"])), out)
    r = run_bass_kernel_spmd(nc, [arrays], core_ids=[0])
    return r.results[0]["out_y"]
```
